# Optimizing a Trainium2 kernel written in Bass

```python
import numpy as np
import jax
import jax.numpy as jnp

def _softmax(x, axis=-1):
    return jax.nn.softmax(x, axis=axis)

def _gelu(x):
    return jax.nn.gelu(x, approximate=True)

def _silu(x):
    return jax.nn.silu(x)

def _sigmoid(x):
    return jax.nn.sigmoid(x)

def _layernorm(x, axis=-1, eps=1e-05):
    m = jnp.mean(x, axis=axis, keepdims=True)
    v = jnp.var(x, axis=axis, keepdims=True)
    return (x - m) / jnp.sqrt(v + eps)

def _scatter_add(tgt, idx, src, axis=0):
    return tgt.at[idx].add(src)

def _segment_sum(src, seg, n):
    return jax.ops.segment_sum(src, seg, n)
kernel_name = 'mk_cond_seq_d1_seqx_r8_8a38e0'

def setup_inputs(seed: int=0):
    np.random.seed(seed)
    _w = jnp.asarray

    def _rec_inputs():
        import jax
        import jax.numpy as jnp
        _rk = jax.random.key(seed)
        x = 7.22e-05 + 1 * jax.random.normal(jax.random.fold_in(_rk, 1), (128, 32, 128), jnp.float32)
        _lenS = 32 - jax.random.randint(jax.random.fold_in(_rk, 7), (128,), 0, max(1, 32 // 4) + 1, jnp.int32)
        _lenS2 = 32 - jax.random.randint(jax.random.fold_in(_rk, 8), (128,), 0, max(1, 32 // 4) + 1, jnp.int32)
        cond_1024 = 0.0061147 + 1.02565 * jax.random.normal(jax.random.fold_in(_rk, 11), (128, 128), jnp.float32)
        return (x, cond_1024)
    x, cond_1024 = _rec_inputs()

    def _L0_cond_setup():
        import jax, jax.numpy as jnp
        import numpy as np
        B, L, D, NH, MLP = (4, 256, 128, 16, 512)
        KD = D // NH
        EPS = 1e-05

        def layer_norm(x, scale=None):
            mu = jnp.mean(x, axis=-1, keepdims=True)
            var = jnp.var(x, axis=-1, keepdims=True)
            y = (x - mu) * jax.lax.rsqrt(var + EPS)
            return y * scale if scale is not None else y

        def rotary_pos_emb(x):
            dim, seq = (x.shape[-1], x.shape[-2])
            inv_freqs = 10000.0 ** (-jnp.arange(0, dim, 2, dtype=jnp.float32) / dim)
            grid = jnp.arange(seq, dtype=jnp.float32)[:, None] * inv_freqs[None, :]
            sin = jnp.repeat(jnp.sin(grid), 2, axis=-1)
            cos = jnp.repeat(jnp.cos(grid), 2, axis=-1)
            x1, x2 = (x[..., ::2], x[..., 1::2])
            xs = jnp.stack([-x2, x1], axis=-1).reshape(x.shape)
            return x * cos + xs * sin
        key = jax.random.key(seed)
        ks = jax.random.split(key, 11)

        def lin(k, fan_in, fan_out):
            return jax.random.normal(k, (fan_in, fan_out), jnp.float32) / np.sqrt(fan_in)
        return {'x': jax.random.normal(ks[0], (B, L, D), jnp.float32), 't_emb': jax.random.normal(ks[1], (B, 1, D), jnp.float32), 'w_scale': lin(ks[2], D, D), 'w_offset': lin(ks[3], D, D), 'wq': lin(ks[4], D, D), 'wk': lin(ks[5], D, D), 'wv': lin(ks[6], D, D), 'wo': lin(ks[7], D, D), 'mlp_ln_scale': jnp.ones((D,), jnp.float32), 'w1': lin(ks[8], D, MLP), 'w2': lin(ks[9], MLP, D)}
    _L0_cond_all = _L0_cond_setup()
    _L0_cond_in = {k: v for k, v in _L0_cond_all.items() if k in ('w_scale', 'w_offset', 'wq', 'wk', 'wv', 'wo', 'mlp_ln_scale', 'w1', 'w2')}
    del _L0_cond_all
    return {'x': x, 'cond_1024': cond_1024, 'L0_cond_w_scale': _L0_cond_in['w_scale'], 'L0_cond_w_offset': _L0_cond_in['w_offset'], 'L0_cond_wq': _L0_cond_in['wq'], 'L0_cond_wk': _L0_cond_in['wk'], 'L0_cond_wv': _L0_cond_in['wv'], 'L0_cond_wo': _L0_cond_in['wo'], 'L0_cond_mlp_ln_scale': _L0_cond_in['mlp_ln_scale'], 'L0_cond_w1': _L0_cond_in['w1'], 'L0_cond_w2': _L0_cond_in['w2']}

def reference(x, cond_1024, L0_cond_w_scale, L0_cond_w_offset, L0_cond_wq, L0_cond_wk, L0_cond_wv, L0_cond_wo, L0_cond_mlp_ln_scale, L0_cond_w1, L0_cond_w2):
    import jax
    import jax.numpy as jnp

    def _L0_cond_ref(x, t_emb, w_scale, w_offset, wq, wk, wv, wo, mlp_ln_scale, w1, w2):
        import jax, jax.numpy as jnp
        import numpy as np
        B, L, D, NH, MLP = (4, 256, 128, 16, 512)
        KD = D // NH
        EPS = 1e-05

        def layer_norm(x, scale=None):
            mu = jnp.mean(x, axis=-1, keepdims=True)
            var = jnp.var(x, axis=-1, keepdims=True)
            y = (x - mu) * jax.lax.rsqrt(var + EPS)
            return y * scale if scale is not None else y

        def rotary_pos_emb(x):
            dim, seq = (x.shape[-1], x.shape[-2])
            inv_freqs = 10000.0 ** (-jnp.arange(0, dim, 2, dtype=jnp.float32) / dim)
            grid = jnp.arange(seq, dtype=jnp.float32)[:, None] * inv_freqs[None, :]
            sin = jnp.repeat(jnp.sin(grid), 2, axis=-1)
            cos = jnp.repeat(jnp.cos(grid), 2, axis=-1)
            x1, x2 = (x[..., ::2], x[..., 1::2])
            xs = jnp.stack([-x2, x1], axis=-1).reshape(x.shape)
            return x * cos + xs * sin
        b, l, d = x.shape
        scale = t_emb @ w_scale
        offset = t_emb @ w_offset
        h = layer_norm(x) * scale + offset
        q = h @ wq / jnp.sqrt(jnp.asarray(d, h.dtype))
        q = q.reshape(b, l, NH, KD).transpose(0, 2, 1, 3)
        k = (h @ wk).reshape(b, l, NH, KD).transpose(0, 2, 1, 3)
        v = (h @ wv).reshape(b, l, NH, KD).transpose(0, 2, 1, 3)
        q = rotary_pos_emb(q)
        k = rotary_pos_emb(k)
        logits = jnp.einsum('bhik,bhjk->bhij', q, k)
        a = jax.nn.softmax(logits, axis=-1)
        y = jnp.einsum('bhij,bhjv->bhiv', a, v)
        y = y.transpose(0, 2, 1, 3).reshape(b, l, d)
        x = x + y @ wo
        h2 = layer_norm(x, mlp_ln_scale)
        h2 = jax.nn.gelu(h2 @ w1) @ w2
        return x + h2
    x = _L0_cond_ref(x, cond_1024[:, None, :], L0_cond_w_scale, L0_cond_w_offset, L0_cond_wq, L0_cond_wk, L0_cond_wv, L0_cond_wo, L0_cond_mlp_ln_scale, L0_cond_w1, L0_cond_w2)
    return x

_drawn_inputs = setup_inputs


def setup_inputs(seed=0):
    import zlib

    import numpy as np

    out = dict(_drawn_inputs(seed))
    spreads = {'L0_cond_mlp_ln_scale': (1.0, 0.2)}
    factors = {}
    for name, (base, spread) in spreads.items():
        noise = np.random.default_rng([zlib.crc32(name.encode()), seed]).standard_normal(out[name].shape)
        drawn = base * np.exp(spread * noise) if base else spread * noise
        out[name] = jnp.asarray(drawn.astype(out[name].dtype))
    for name, factor in factors.items():
        out[name] = (out[name] * factor).astype(out[name].dtype)
    return out
```

```python
from contextlib import ExitStack

import numpy as np

import concourse.bass as bass
from concourse import mybir

F32 = mybir.dt.float32
ALU = mybir.AluOpType
ACT = mybir.ActivationFunctionType
AX_X = mybir.AxisListType.X

P = 128
BATCH, SEQ, DIM = 128, 32, 128
HEADS = 16
HEAD_DIM = DIM // HEADS
HALF = HEAD_DIM // 2
HIDDEN = 512
CHUNKS = HIDDEN // P
EPS = 1e-5
TILE_BATCHES = P // SEQ
TILES = BATCH * SEQ // P
ST = 4
STEPS = TILES // ST
ST_TOKENS = ST * P
ST_BATCHES = ST * TILE_BATCHES
V_COLS = HEAD_DIM + 1
V_BLOCK = HEADS * V_COLS
ACT_HEADS = 7


def build(nc, x, cond, w_scale, w_offset, wqk, wv, wo, ln_scale, w1, w2, rope, head_mask, identity, out):
    ctx = ExitStack()
    with ctx:
        def sb(name, shape):
            return ctx.enter_context(nc.sbuf_tensor(name, shape, F32))

        def pb(name, cols):
            return ctx.enter_context(nc.psum_tensor(name, [P, cols], F32))

        def sem(name):
            return ctx.enter_context(nc.semaphore(name))

        x_sb = sb("x_sb", [P, TILES, DIM])
        x1_sb = sb("x1_sb", [P, TILES, DIM])
        cond_sb = sb("cond_sb", [P, DIM])
        wsc_sb = sb("wsc_sb", [P, DIM])
        wof_sb = sb("wof_sb", [P, DIM])
        wqk_sb = sb("wqk_sb", [P, 2 * DIM])
        wv_sb = sb("wv_sb", [P, DIM])
        wo_sb = sb("wo_sb", [P, DIM])
        lns_sb = sb("lns_sb", [P, 1])
        w1_sb = sb("w1_sb", [P, HIDDEN])
        w1s_sb = sb("w1s_sb", [P, HIDDEN])
        w2_sb = sb("w2_sb", [P, CHUNKS, DIM])
        rope_sb = sb("rope_sb", [P, 2, HEAD_DIM])
        mask_sb = sb("mask_sb", [P, HEADS])
        ident = sb("ident", [P, P])
        condT = sb("condT", [P, BATCH])
        scaleT = sb("scaleT", [P, BATCH])
        offT = sb("offT", [P, BATCH])
        eps_sb = sb("eps_sb", [P, ST])
        half_neg = sb("half_neg", [P, ST])
        stats = [sb(f"stats{u}", [P, ST, 6]) for u in range(2)]
        mv = [sb(f"mv{u}", [P, ST, 2]) for u in range(2)]
        veps = [sb(f"veps{u}", [P, ST]) for u in range(2)]
        rstd = [sb(f"rstd{u}", [P, ST]) for u in range(2)]
        xn = sb("xn", [P, ST, DIM])
        hs = sb("hs", [P, ST_TOKENS])
        hT = [sb(f"hT{u}", [P, ST_TOKENS]) for u in range(2)]
        rope_a = sb("rope_a", [P, ST * 2 * DIM])
        rope_b = sb("rope_b", [P, ST * 2 * DIM])
        qk_rot = sb("qk_rot", [P, ST * 2 * DIM])
        qT = [sb(f"qT{u}", [P, ST_TOKENS]) for u in range(2)]
        kT = sb("kT", [P, ST_TOKENS])
        k_spread = [sb(f"k_spread{u}", [P, HEADS, ST_TOKENS]) for u in range(2)]
        v_diag = [sb(f"v_diag{u}", [P, ST, TILE_BATCHES, HEADS, V_COLS]) for u in range(2)]
        neg_max = [sb(f"neg_max{u}", [P, HEADS]) for u in range(2)]
        shifted = [sb(f"shifted{u}", [P, HEADS * SEQ]) for u in range(2)]
        expd = [sb(f"expd{u}", [P, HEADS * SEQ]) for u in range(2)]
        eT = [sb(f"eT{u}", [P, HEADS * SEQ]) for u in range(2)]
        recip = sb("recip", [P, ST * HEADS])
        y_sb = sb("y_sb", [P, ST_TOKENS])
        yT = sb("yT", [P, ST_TOKENS])
        gelu = [sb(f"gelu{u}", [P, CHUNKS, ST_TOKENS]) for u in range(2)]

        bank_t = pb("bank_t", 512)
        bank_v = pb("bank_v", 512)
        bank_qk = pb("bank_qk", 1024)
        bank_log = [pb(f"bank_log{u}", 512) for u in range(2)]
        bank_pv = [pb(f"bank_pv{u}", 512) for u in range(2)]
        hidden_bank = [bank_qk[:, 0:512], bank_qk[:, 512:1024], bank_log[0][:, :], bank_log[1][:, :]]

        s_x_first = sem("x_first")
        s_x_rest = sem("x_rest")
        s_setup = sem("setup_loaded")
        s_attn_w = sem("attn_weights_loaded")
        s_mlp_w = sem("mlp_weights_loaded")
        s_half = sem("exponent_set")
        s_vzero = sem("v_diag_zeroed")
        s_vones = sem("v_diag_ones")
        s_condT_ps = sem("condT_in_psum")
        s_condT = sem("condT_ready")
        s_mod_ps = sem("modulation_in_psum")
        s_mod = sem("modulation_ready")
        s_w1s = sem("w1_scaled")
        s_stats = sem("stats_done")
        s_mv = sem("mean_var_done")
        s_veps = sem("var_eps_done")
        s_rstd = sem("rstd_ready")
        s_xn = sem("normed_ready")
        s_xnT = sem("normedT_in_psum")
        s_hs = sem("scaled_ready")
        s_hT = sem("hT_ready")
        s_qk = sem("qk_in_psum")
        s_v = sem("v_in_psum")
        s_rope = sem("rope_products_ready")
        s_rot = sem("qk_rotated")
        s_qkT = sem("qkT_in_psum")
        s_qT = sem("qT_ready")
        s_kT = sem("kT_ready")
        s_spread_a = sem("k_spread_by_act")
        s_spread_p = sem("k_spread_by_pool")
        s_vd = sem("v_diag_ready")
        s_log = sem("logits_in_psum")
        s_max = sem("max_done")
        s_shift = sem("logits_shifted")
        s_exp = sem("exp_done")
        s_eT = sem("expT_ready")
        s_pv = sem("pv_in_psum")
        s_recip = sem("recip_done")
        s_y = sem("y_normalised")
        s_yT = sem("yT_ready")
        s_wo = sem("proj_in_psum")
        s_x1 = sem("x1_ready")
        b_stats = sem("mlp_stats_done")
        b_mv = sem("mlp_mean_var_done")
        b_veps = sem("mlp_var_eps_done")
        b_rstd = sem("mlp_rstd_ready")
        b_n = sem("mlp_normed_ready")
        b_nT_ps = sem("mlp_normedT_in_psum")
        b_nT = sem("mlp_normedT_ready")
        b_h = sem("hidden_in_psum")
        b_g = sem("gelu_ready")
        b_o = sem("mlp_out_in_psum")
        b_res = sem("result_ready")
        s_store = sem("result_stored")

        x_t = x.rearrange("(t b) l d -> (b l) t d", b=TILE_BATCHES)
        out_t = out.rearrange("(t b) l d -> (b l) t d", b=TILE_BATCHES)

        block = ctx.enter_context(nc.Block())

        @block.sync
        def _(sp):
            sp.dma_start(x_sb[:, 0:ST, :], x_t[:, 0:ST, :]).then_inc(s_x_first, 16)
            sp.dma_start(ident[:, :], identity).then_inc(s_setup, 16)
            sp.dma_start(cond_sb[:, :], cond).then_inc(s_setup, 16)
            sp.dma_start(wsc_sb[:, :], w_scale).then_inc(s_setup, 16)
            sp.dma_start(wof_sb[:, :], w_offset).then_inc(s_setup, 16)
            sp.dma_start(wqk_sb[:, :], wqk).then_inc(s_attn_w, 16)
            sp.dma_start(wv_sb[:, :], wv).then_inc(s_attn_w, 16)
            sp.dma_start(rope_sb[:, :, :], rope).then_inc(s_attn_w, 16)
            sp.dma_start(mask_sb[:, :], head_mask).then_inc(s_attn_w, 16)
            sp.dma_start(wo_sb[:, :], wo).then_inc(s_attn_w, 16)
            sp.dma_start(x_sb[:, ST:TILES, :], x_t[:, ST:TILES, :]).then_inc(s_x_rest, 16)
            sp.dma_start(w1_sb[:, :], w1).then_inc(s_mlp_w, 16)
            sp.dma_start(lns_sb[:, :], ln_scale).then_inc(s_mlp_w, 16)
            sp.dma_start(w2_sb[:, :, :], w2.rearrange("(c p) n -> p c n", p=P)).then_inc(s_mlp_w, 16)
            with sp.Fori(0, STEPS) as g:
                sp.wait_ge(b_res, g + 1)
                sp.dma_start(out_t[:, bass.ds(ST * g, ST), :],
                             x1_sb[:, bass.ds(ST * g, ST), :]).then_inc(s_store, 16)
            sp.wait_ge(s_store, 16 * STEPS)

        @block.vector
        def _(dve):
            def norm_stats(src, m, u, stats_sem):
                for t in range(ST):
                    last = nc.vector.bn_stats(stats[u][:, t, :], src[:, ST * m + t, :])
                last.then_inc(stats_sem, 1)

            def norm_aggregate(u, mv_sem):
                for t in range(ST):
                    last = nc.vector.bn_aggr(mv[u][:, t, :], stats[u][:, t, :])
                last.then_inc(mv_sem, 1)

            def normalise(m, u):
                dve.wait_ge(s_rstd, m + 1)
                dve.wait_ge(s_xnT, m)
                for t in range(ST):
                    last = nc.vector.tensor_scalar(xn[:, t, :], x_sb[:, ST * m + t, :], mv[u][:, t, 0:1],
                                                   rstd[u][:, t:t + 1], ALU.subtract, ALU.mult)
                last.then_inc(s_xn, 1)

            def modulate(m):
                dve.wait_ge(s_xnT, m + 1)
                dve.wait_ge(s_hT, m)
                nc.vector.tensor_tensor(
                    hs[:, :].rearrange("p (b l) -> p b l", l=SEQ),
                    bank_t[:, :].rearrange("p (b l) -> p b l", l=SEQ),
                    scaleT[:, bass.ds(ST_BATCHES * m, ST_BATCHES)].unsqueeze(2).to_broadcast([P, ST_BATCHES, SEQ]),
                    ALU.mult).then_inc(s_hs, 1)

            def rotate(m):
                n = ST * 2 * HEADS
                src = bank_qk[:, :].rearrange("p (n d) -> p n d", d=HEAD_DIM)
                a = rope_a[:, :].rearrange("p (n d) -> p n d", d=HEAD_DIM)
                b = rope_b[:, :].rearrange("p (n d) -> p n d", d=HEAD_DIM)
                dve.wait_ge(s_qk, m + 1)
                dve.wait_ge(s_rot, m)
                nc.vector.tensor_tensor(a, src, rope_sb[:, 0:1, :].to_broadcast([P, n, HEAD_DIM]), ALU.mult)
                nc.vector.tensor_tensor(b[:, :, 0:HALF], src[:, :, HALF:HEAD_DIM],
                                        rope_sb[:, 1:2, 0:HALF].to_broadcast([P, n, HALF]), ALU.mult)
                nc.vector.tensor_tensor(b[:, :, HALF:HEAD_DIM], src[:, :, 0:HALF],
                                        rope_sb[:, 1:2, HALF:HEAD_DIM].to_broadcast([P, n, HALF]),
                                        ALU.mult).then_inc(s_rope, 1)

            def shift(m, t, aggregate_m=None, aggregate_u=None):
                src = bank_log[t % 2][:, :].rearrange("p (h k) -> p h k", k=SEQ)
                if aggregate_m is not None:
                    dve.wait_ge(s_stats, aggregate_m + 1)
                dve.wait_ge(s_log, ST * m + t + 1)
                nc.vector.tensor_reduce(neg_max[t % 2][:, :], src, axis=AX_X, op=ALU.max,
                                        negate=True).then_inc(s_max, 1)
                if aggregate_m is not None:
                    norm_aggregate(aggregate_u, s_mv)
                if t >= 2:
                    dve.wait_ge(s_exp, ST * m + t - 1)
                else:
                    dve.wait_ge(s_exp, ST * m)
                dve.wait_ge(s_max, ST * m + t + 1)
                nc.vector.tensor_tensor(shifted[t % 2][:, :].rearrange("p (h k) -> p h k", k=SEQ), src,
                                        neg_max[t % 2][:, :].unsqueeze(2).to_broadcast([P, HEADS, SEQ]),
                                        ALU.add).then_inc(s_shift, 1)

            def transpose_exp(m, t):
                dve.wait_ge(s_exp, ST * m + t + 1)
                if t >= 2:
                    dve.wait_ge(s_pv, ST * m + t - 1)
                else:
                    dve.wait_ge(s_pv, ST * m)
                nc.vector.transpose(eT[t % 2][:, :], expd[t % 2][:, :]).then_inc(s_eT, 1)

            def divide(m, pair):
                n = 2 * TILE_BATCHES * 4
                src = bank_pv[pair][:, 0:n * V_COLS].rearrange("p (n c) -> p n c", c=V_COLS)
                rec = recip[:, n * pair:n * (pair + 1)]
                dve.wait_ge(s_pv, ST * m + 2 * pair + 2)
                nc.vector.reciprocal(rec.unsqueeze(2), src[:, :, HEAD_DIM:V_COLS]).then_inc(s_recip, 1)
                dve.wait_ge(s_recip, 2 * m + pair + 1)
                nc.vector.tensor_tensor(
                    y_sb[:, 2 * P * pair:2 * P * (pair + 1)].rearrange("p (n d) -> p n d", d=HEAD_DIM),
                    src[:, :, 0:HEAD_DIM], rec.unsqueeze(2).to_broadcast([P, n, HEAD_DIM]),
                    ALU.mult).then_inc(s_y, 1)

            def transpose_y(m):
                dve.wait_ge(s_y, 2 * m + 2)
                dve.wait_ge(s_wo, m)
                nc.vector.transpose(yT[:, :], y_sb[:, :]).then_inc(s_yT, 1)

            def residual(m):
                dve.wait_ge(s_wo, m + 1)
                nc.vector.tensor_tensor(x1_sb[:, bass.ds(ST * m, ST), :],
                                        bank_t[:, :].rearrange("p (t d) -> p t d", d=DIM),
                                        x_sb[:, bass.ds(ST * m, ST), :], ALU.add).then_inc(s_x1, 1)

            def body(m, u, ahead1, ahead2):
                if ahead2:
                    norm_stats(x_sb, m + 2, u, s_stats)
                    shift(m, 0, m + 2, u)
                    normalise(m + 2, u)
                else:
                    shift(m, 0)
                shift(m, 1)
                transpose_exp(m, 0)
                shift(m, 2)
                transpose_exp(m, 1)
                if ahead2:
                    modulate(m + 2)
                shift(m, 3)
                transpose_exp(m, 2)
                divide(m, 0)
                transpose_exp(m, 3)
                divide(m, 1)
                transpose_y(m)
                if ahead2:
                    rotate(m + 2)
                residual(m)

            nc.vector.memset(eps_sb[:, :], EPS).then_inc(s_half, 1)
            nc.vector.memset(half_neg[:, :], -0.5).then_inc(s_half, 1)
            for u in range(2):
                nc.vector.memset(v_diag[u][:, :, :, :, :], 0.0).then_inc(s_vzero, 1)
            dve.wait_ge(s_x_first, 16)
            norm_stats(x_sb, 0, 0, s_stats)
            dve.wait_ge(s_stats, 1)
            norm_aggregate(0, s_mv)
            dve.wait_ge(s_vzero, 2)
            for u in range(2):
                for b in range(TILE_BATCHES):
                    last = nc.vector.memset(
                        v_diag[u][SEQ * b:SEQ * (b + 1), :, b, :, HEAD_DIM:V_COLS], 1.0)
            last.then_inc(s_vones, 1)
            dve.wait_ge(s_condT_ps, 1)
            nc.vector.tensor_copy(condT[:, :], bank_pv[0][:, 0:BATCH]).then_inc(s_condT, 1)
            normalise(0, 0)
            dve.wait_ge(s_mod_ps, 2)
            nc.vector.tensor_copy(scaleT[:, :], bank_pv[0][:, 0:BATCH]).then_inc(s_mod, 1)
            nc.vector.tensor_copy(offT[:, :], bank_pv[0][:, BATCH:2 * BATCH]).then_inc(s_mod, 1)
            dve.wait_ge(s_mod, 2)
            modulate(0)
            dve.wait_ge(s_x_rest, 16)
            norm_stats(x_sb, 1, 1, s_stats)
            dve.wait_ge(s_stats, 2)
            norm_aggregate(1, s_mv)
            dve.wait_ge(s_attn_w, 80)
            rotate(0)
            normalise(1, 1)
            modulate(1)
            rotate(1)
            for m in range(2):
                body(m, m, True, True)
            with dve.Fori(1, STEPS // 2 - 1) as i:
                for u in range(2):
                    body(2 * i + u, u, True, True)
            body(STEPS - 2, 0, True, False)
            body(STEPS - 1, 1, False, False)

            def mlp_normalise(g, u):
                dve.wait_ge(b_rstd, g + 1)
                dve.wait_ge(b_nT_ps, g)
                for t in range(ST):
                    last = nc.vector.tensor_scalar(xn[:, t, :], x1_sb[:, ST * g + t, :], mv[u][:, t, 0:1],
                                                   rstd[u][:, t:t + 1], ALU.subtract, ALU.mult)
                last.then_inc(b_n, 1)

            def mlp_norm(g, u):
                norm_stats(x1_sb, g, u, b_stats)
                dve.wait_ge(b_stats, g + 1)
                norm_aggregate(u, b_mv)
                mlp_normalise(g, u)

            def mlp_residual(g, u):
                dve.wait_ge(b_o, g + 1)
                nc.vector.tensor_tensor(x1_sb[:, bass.ds(ST * g, ST), :], bank_pv[u][:, :].rearrange("p (t d) -> p t d", d=DIM),
                                        x1_sb[:, bass.ds(ST * g, ST), :], ALU.add).then_inc(b_res, 1)

            dve.wait_ge(s_mlp_w, 48)
            nc.vector.tensor_scalar(w1s_sb[:, :], w1_sb[:, :], lns_sb[:, 0:1], None, ALU.mult).then_inc(s_w1s, 1)
            dve.wait_ge(s_x1, STEPS)
            for g in range(3):
                mlp_norm(g, g % 2)
            with dve.Fori(0, STEPS // 2 - 2) as i:
                for u in range(2):
                    g = 2 * i + u
                    norm_stats(x1_sb, g + 3, 1 - u, b_stats)
                    dve.wait_ge(b_stats, g + 4)
                    mlp_residual(g, u)
                    norm_aggregate(1 - u, b_mv)
                    mlp_normalise(g + 3, 1 - u)
            mlp_norm(STEPS - 1, 1)
            for g in range(STEPS - 4, STEPS):
                mlp_residual(g, g % 2)

        @block.gpsimd
        def _(pool):
            def inv_sigma(m, u, mv_sem, veps_sem, rstd_sem):
                pool.wait_ge(mv_sem, m + 1)
                nc.gpsimd.tensor_tensor(veps[u][:, :].unsqueeze(2), mv[u][:, :, 1:2], eps_sb[:, :].unsqueeze(2),
                                        ALU.add).then_inc(veps_sem, 1)
                pool.wait_ge(veps_sem, m + 1)
                nc.gpsimd.tensor_tensor(rstd[u][:, :], veps[u][:, :], half_neg[:, :], ALU.pow).then_inc(rstd_sem, 1)

            def add_offset(m, u, reuse):
                pool.wait_ge(s_hs, m + 1)
                if reuse:
                    pool.wait_ge(s_v, m - 1)
                nc.gpsimd.tensor_tensor(
                    hT[u][:, :].rearrange("p (b l) -> p b l", l=SEQ),
                    hs[:, :].rearrange("p (b l) -> p b l", l=SEQ),
                    offT[:, bass.ds(ST_BATCHES * m, ST_BATCHES)].unsqueeze(2).to_broadcast([P, ST_BATCHES, SEQ]),
                    ALU.add).then_inc(s_hT, 1)

            def rotate_add(m):
                pool.wait_ge(s_rope, m + 1)
                pool.wait_ge(s_qkT, m)
                nc.gpsimd.tensor_tensor(qk_rot[:, :], rope_a[:, :], rope_b[:, :], ALU.add).then_inc(s_rot, 1)

            def spread(m, u, first, last_head, reuse):
                if first == ACT_HEADS:
                    pool.wait_ge(s_kT, m + 1)
                    if reuse:
                        pool.wait_ge(s_log, ST * (m - 1))
                    last = nc.gpsimd.tensor_tensor(k_spread[u][:, first, :], kT[:, :],
                                                   mask_sb[:, first:first + 1].to_broadcast([P, ST_TOKENS]), ALU.mult)
                    first += 1
                for h in range(first, last_head):
                    last = nc.gpsimd.tensor_scalar(k_spread[u][:, h, :], kT[:, :], mask_sb[:, h:h + 1], 0.0,
                                                   ALU.mult, ALU.add)
                if last_head == HEADS:
                    last.then_inc(s_spread_p, 1)

            mid = (ACT_HEADS + HEADS) // 2
            pool.wait_ge(s_half, 2)
            inv_sigma(0, 0, s_mv, s_veps, s_rstd)
            pool.wait_ge(s_mod, 2)
            add_offset(0, 0, False)
            inv_sigma(1, 1, s_mv, s_veps, s_rstd)
            rotate_add(0)
            add_offset(1, 1, False)
            pool.wait_ge(s_attn_w, 80)
            spread(0, 0, ACT_HEADS, HEADS, False)

            def body(m, u, reuse):
                rotate_add(m + 1)
                inv_sigma(m + 2, u, s_mv, s_veps, s_rstd)
                spread(m + 1, 1 - u, ACT_HEADS, mid, reuse)
                add_offset(m + 2, u, True)
                spread(m + 1, 1 - u, mid, HEADS, reuse)

            for m in range(2):
                body(m, m, m > 0)
            with pool.Fori(1, STEPS // 2 - 1) as i:
                for u in range(2):
                    body(2 * i + u, u, True)
            rotate_add(STEPS - 1)
            spread(STEPS - 1, 1, ACT_HEADS, HEADS, True)

            with pool.Fori(0, STEPS // 2) as i:
                for u in range(2):
                    inv_sigma(2 * i + u, u, b_mv, b_veps, b_rstd)

        @block.scalar
        def _(act):
            def place_v(m, u, reuse):
                act.wait_ge(s_v, m + 1)
                if reuse:
                    act.wait_ge(s_pv, ST * (m - 1))
                for b in range(TILE_BATCHES):
                    rows = slice(SEQ * b, SEQ * (b + 1))
                    last = nc.scalar.activation(
                        v_diag[u][rows, :, b, :, 0:HEAD_DIM],
                        bank_v[rows, :].rearrange("p (t h d) -> p t h d", h=HEADS, d=HEAD_DIM), ACT.Copy)
                last.then_inc(s_vd, 1)

            def evict_qkT(m, u, reuse):
                act.wait_ge(s_qkT, m + 1)
                if reuse:
                    act.wait_ge(s_log, ST * (m - 1))
                nc.scalar.activation(qT[u][:, :], bank_qk[:, 0:512], ACT.Copy,
                                     scale=float(DIM) ** -0.5).then_inc(s_qT, 1)
                act.wait_ge(s_spread_p, m)
                act.wait_ge(s_spread_a, m)
                nc.scalar.activation(kT[:, :], bank_qk[:, 512:1024], ACT.Copy).then_inc(s_kT, 1)

            def spread(m, u, first, last_head):
                if first == 0:
                    act.wait_ge(s_kT, m + 1)
                for h in range(first, last_head):
                    last = nc.scalar.activation(k_spread[u][:, h, :], kT[:, :], ACT.Copy,
                                                scale=mask_sb[:, h:h + 1])
                if last_head == ACT_HEADS:
                    last.then_inc(s_spread_a, 1)

            def exponentiate(m, t):
                act.wait_ge(s_shift, ST * m + t + 1)
                if t >= 2:
                    act.wait_ge(s_eT, ST * m + t - 1)
                else:
                    act.wait_ge(s_eT, ST * m)
                nc.scalar.activation(expd[t % 2][:, :], shifted[t % 2][:, :], ACT.Exp).then_inc(s_exp, 1)

            mid = ACT_HEADS // 2
            act.wait_ge(s_vones, 1)
            place_v(0, 0, False)
            act.wait_ge(s_attn_w, 80)
            evict_qkT(0, 0, False)
            spread(0, 0, 0, ACT_HEADS)
            def body(m, u, reuse):
                exponentiate(m, 0)
                place_v(m + 1, 1 - u, reuse)
                exponentiate(m, 1)
                evict_qkT(m + 1, 1 - u, reuse)
                spread(m + 1, 1 - u, 0, mid)
                exponentiate(m, 2)
                spread(m + 1, 1 - u, mid, ACT_HEADS)
                exponentiate(m, 3)

            for m in range(2):
                body(m, m, m > 0)
            with act.Fori(1, STEPS // 2 - 1) as i:
                for u in range(2):
                    body(2 * i + u, u, True)
            body(STEPS - 2, 0, True)
            for t in range(ST):
                exponentiate(STEPS - 1, t)

            def evict_nT(g):
                act.wait_ge(b_nT_ps, g + 1)
                act.wait_ge(b_h, CHUNKS * g)
                nc.scalar.activation(hT[0][:, :], bank_t[:, :], ACT.Copy).then_inc(b_nT, 1)

            def gelus(g, u, reuse):
                for c in range(CHUNKS):
                    act.wait_ge(b_h, CHUNKS * g + c + 1)
                    if reuse and c == 0:
                        act.wait_ge(b_o, g - 1)
                    nc.scalar.activation(gelu[u][:, c, :], hidden_bank[c], ACT.Gelu_apprx_tanh).then_inc(b_g, 1)

            act.wait_ge(s_v, STEPS)
            evict_nT(0)
            gelus(0, 0, False)
            evict_nT(1)
            gelus(1, 1, False)
            with act.Fori(1, STEPS // 2) as i:
                for u in range(2):
                    evict_nT(2 * i + u)
                    gelus(2 * i + u, u, True)

        @block.tensor
        def _(pe):
            def transpose_norm(m, reuse):
                pe.wait_ge(s_xn, m + 1)
                pe.wait_ge(s_hs, m)
                if reuse:
                    pe.wait_ge(s_x1, m - 2)
                for t in range(ST):
                    last = nc.tensor.transpose(bank_t[:, P * t:P * (t + 1)], xn[:, t, :], ident[:, :])
                last.then_inc(s_xnT, 1)

            def project(m, u):
                pe.wait_ge(s_hT, m + 1)
                pe.wait_ge(s_kT, m)
                pe.wait_ge(s_qT, m)
                for t in range(ST):
                    last = nc.tensor.matmul(bank_qk[:, 2 * DIM * t:2 * DIM * (t + 1)], hT[u][:, P * t:P * (t + 1)],
                                            wqk_sb[:, :], start=True, stop=True)
                last.then_inc(s_qk, 1)
                pe.wait_ge(s_vd, m)
                for t in range(ST):
                    last = nc.tensor.matmul(bank_v[:, DIM * t:DIM * (t + 1)], hT[u][:, P * t:P * (t + 1)],
                                            wv_sb[:, :], start=True, stop=True)
                last.then_inc(s_v, 1)

            def transpose_qk(m):
                pe.wait_ge(s_rot, m + 1)
                for j in range(2):
                    for t in range(ST):
                        c = 2 * DIM * t + DIM * j
                        last = nc.tensor.transpose(bank_qk[:, 512 * j + P * t:512 * j + P * (t + 1)],
                                                   qk_rot[:, c:c + DIM], ident[:, :])
                last.then_inc(s_qkT, 1)

            def logits(m, u, t):
                if t == 0:
                    pe.wait_ge(s_qT, m + 1)
                    pe.wait_ge(s_spread_a, m + 1)
                    pe.wait_ge(s_spread_p, m + 1)
                if t >= 2:
                    pe.wait_ge(s_shift, ST * m + t - 1)
                else:
                    pe.wait_ge(s_shift, ST * m)
                for b in range(TILE_BATCHES):
                    c = P * t + SEQ * b
                    last = nc.tensor.matmul(bank_log[t % 2][SEQ * b:SEQ * (b + 1), :], qT[u][:, c:c + SEQ],
                                            k_spread[u][:, :, c:c + SEQ], start=True, stop=True)
                last.then_inc(s_log, 1)

            def weigh(m, u, t):
                if t == 0:
                    pe.wait_ge(s_vd, m + 1)
                    pe.wait_ge(s_y, 2 * m)
                pe.wait_ge(s_eT, ST * m + t + 1)
                for g in range(4):
                    for j in range(4):
                        h = 4 * j + g
                        base = (t % 2) * TILE_BATCHES * 4 * V_COLS
                        dst = bank_pv[t // 2][SEQ * j:SEQ * (j + 1), base:base + TILE_BATCHES * 4 * V_COLS]
                        dst = dst.rearrange("p (b g c) -> p b g c", b=TILE_BATCHES, g=4)[:, :, g, :]
                        last = nc.tensor.matmul(dst, eT[t % 2][:, SEQ * h:SEQ * (h + 1)],
                                                v_diag[u][:, t, :, h, :], start=True, stop=True)
                last.then_inc(s_pv, 1)

            def project_out(m, ahead2):
                pe.wait_ge(s_yT, m + 1)
                if ahead2:
                    pe.wait_ge(s_hs, m + 3)
                else:
                    pe.wait_ge(s_x1, m)
                for t in range(ST):
                    last = nc.tensor.matmul(bank_t[:, DIM * t:DIM * (t + 1)], yT[:, P * t:P * (t + 1)],
                                            wo_sb[:, :], start=True, stop=True)
                last.then_inc(s_wo, 1)

            def body(m, u, ahead1, ahead2):
                logits(m, u, 0)
                logits(m, u, 1)
                if ahead1:
                    transpose_qk(m + 1)
                weigh(m, u, 0)
                logits(m, u, 2)
                if ahead2:
                    transpose_norm(m + 2, True)
                weigh(m, u, 1)
                logits(m, u, 3)
                weigh(m, u, 2)
                weigh(m, u, 3)
                if ahead2:
                    project(m + 2, u)
                project_out(m, ahead2)

            pe.wait_ge(s_setup, 64)
            nc.tensor.transpose(bank_pv[0][:, 0:BATCH], cond_sb[:, :], ident[:, :]).then_inc(s_condT_ps, 1)
            pe.wait_ge(s_condT, 1)
            nc.tensor.matmul(bank_pv[0][:, 0:BATCH], wsc_sb[:, :], condT[:, :], start=True,
                             stop=True).then_inc(s_mod_ps, 1)
            nc.tensor.matmul(bank_pv[0][:, BATCH:2 * BATCH], wof_sb[:, :], condT[:, :], start=True,
                             stop=True).then_inc(s_mod_ps, 1)
            transpose_norm(0, False)
            pe.wait_ge(s_attn_w, 80)
            project(0, 0)
            transpose_norm(1, False)
            transpose_qk(0)
            project(1, 1)
            for m in range(2):
                body(m, m, True, True)
            with pe.Fori(1, STEPS // 2 - 1) as i:
                for u in range(2):
                    body(2 * i + u, u, True, True)
            body(STEPS - 2, 0, True, False)
            body(STEPS - 1, 1, False, False)

            def transpose_mlp_norm(g):
                pe.wait_ge(b_n, g + 1)
                pe.wait_ge(b_nT, g)
                for t in range(ST):
                    last = nc.tensor.transpose(bank_t[:, P * t:P * (t + 1)], xn[:, t, :], ident[:, :])
                last.then_inc(b_nT_ps, 1)

            def hidden(g):
                pe.wait_ge(b_nT, g + 1)
                for c in range(CHUNKS):
                    pe.wait_ge(b_g, CHUNKS * g)
                    nc.tensor.matmul(hidden_bank[c], w1s_sb[:, P * c:P * (c + 1)], hT[0][:, :], start=True,
                                     stop=True).then_inc(b_h, 1)

            def down(g, u, reuse):
                pe.wait_ge(b_g, CHUNKS * (g + 1))
                if reuse:
                    pe.wait_ge(b_res, g - 1)
                for t in range(ST):
                    for c in range(CHUNKS):
                        last = nc.tensor.matmul(bank_pv[u][:, DIM * t:DIM * (t + 1)],
                                                gelu[u][:, c, P * t:P * (t + 1)], w2_sb[:, c, :],
                                                start=(c == 0), stop=(c == CHUNKS - 1))
                last.then_inc(b_o, 1)

            pe.wait_ge(s_mlp_w, 48)
            pe.wait_ge(s_w1s, 1)
            transpose_mlp_norm(0)
            hidden(0)
            transpose_mlp_norm(1)
            for g in range(2):
                hidden(g + 1)
                transpose_mlp_norm(g + 2)
                down(g, g, False)
            with pe.Fori(1, STEPS // 2 - 1) as i:
                for u in range(2):
                    g = 2 * i + u
                    hidden(g + 1)
                    transpose_mlp_norm(g + 2)
                    down(g, u, True)
            hidden(STEPS - 1)
            down(STEPS - 2, 0, True)
            down(STEPS - 1, 1, True)


def _constants():
    freq = 10000.0 ** (-np.arange(0, HEAD_DIM, 2, dtype=np.float32) / HEAD_DIM)
    grid = (np.arange(P, dtype=np.float32) % SEQ)[:, None] * freq[None, :].astype(np.float32)
    cos, sin = np.cos(grid).astype(np.float32), np.sin(grid).astype(np.float32)
    rope = np.stack([np.concatenate([cos, cos], 1), np.concatenate([-sin, sin], 1)], 1)
    mask = (np.arange(P)[:, None] // HEAD_DIM == np.arange(HEADS)[None, :]).astype(np.float32)
    return np.ascontiguousarray(rope, np.float32), mask, np.eye(P, dtype=np.float32)


def kernel(**inputs):
    import concourse.bacc as bacc
    from concourse.bass_utils import run_bass_kernel_spmd as run

    pre = "L0_cond_"
    order = np.concatenate([h * HEAD_DIM + np.concatenate([np.arange(0, HEAD_DIM, 2), np.arange(1, HEAD_DIM, 2)])
                            for h in range(HEADS)])
    wq, wk = (np.asarray(inputs[pre + n])[:, order] for n in ("wq", "wk"))
    rope, mask, eye = _constants()
    arrays = {
        "x_in": np.asarray(inputs["x"]),
        "cond_in": np.asarray(inputs["cond_1024"]),
        "w_scale_in": np.asarray(inputs[pre + "w_scale"]),
        "w_offset_in": np.asarray(inputs[pre + "w_offset"]),
        "wqk_in": np.concatenate([wq, wk], 1),
        "wv_in": np.asarray(inputs[pre + "wv"]),
        "wo_in": np.asarray(inputs[pre + "wo"]),
        "ln_scale_in": np.asarray(inputs[pre + "mlp_ln_scale"]).reshape(DIM, 1),
        "w1_in": np.asarray(inputs[pre + "w1"]),
        "w2_in": np.asarray(inputs[pre + "w2"]),
        "rope_in": rope,
        "head_mask_in": mask,
        "identity_in": eye,
    }
    arrays = {n: np.ascontiguousarray(a) for n, a in arrays.items()}
    nc = bacc.Bacc("TRN2", target_bir_lowering=False, num_devices=1)
    args = [nc.dram_tensor(n, a.shape, mybir.dt.from_np(a.dtype), kind="ExternalInput").ap() for n, a in arrays.items()]
    out = nc.dram_tensor("block_out", (BATCH, SEQ, DIM), F32, kind="ExternalOutput").ap()
    build(nc, *args, out)
    r = run(nc, [arrays], core_ids=[0])
    return r.results[0]["block_out"]
```

```python
from contextlib import ExitStack

import numpy as np

import concourse.bass as bass
from concourse import mybir

F32 = mybir.dt.float32
ALU = mybir.AluOpType
ACT = mybir.ActivationFunctionType
AX_X = mybir.AxisListType.X

P = 128
BATCH, SEQ, DIM = 128, 32, 128
HEADS = 16
HEAD_DIM = DIM // HEADS
HALF = HEAD_DIM // 2
HIDDEN = 512
CHUNKS = HIDDEN // P
EPS = 1e-5
TILE_BATCHES = P // SEQ
TILES = BATCH * SEQ // P
ST = 4
STEPS = TILES // ST
ST_TOKENS = ST * P
ST_BATCHES = ST * TILE_BATCHES
V_COLS = HEAD_DIM + 1
V_BLOCK = HEADS * V_COLS
ACT_HEADS = 7


def build(nc, x, cond, w_scale, w_offset, wqk, wv, wo, ln_scale, w1, w2, rope, head_mask, identity, out):
    ctx = ExitStack()
    with ctx:
        def sb(name, shape):
            return ctx.enter_context(nc.sbuf_tensor(name, shape, F32))

        def pb(name, cols):
            return ctx.enter_context(nc.psum_tensor(name, [P, cols], F32))

        def sem(name):
            return ctx.enter_context(nc.semaphore(name))

        x_sb = sb("x_sb", [P, TILES, DIM])
        x1_sb = sb("x1_sb", [P, TILES, DIM])
        cond_sb = sb("cond_sb", [P, DIM])
        wsc_sb = sb("wsc_sb", [P, DIM])
        wof_sb = sb("wof_sb", [P, DIM])
        wqk_sb = sb("wqk_sb", [P, 2 * DIM])
        wv_sb = sb("wv_sb", [P, DIM])
        wo_sb = sb("wo_sb", [P, DIM])
        lns_sb = sb("lns_sb", [P, 1])
        w1_sb = sb("w1_sb", [P, HIDDEN])
        w1s_sb = sb("w1s_sb", [P, HIDDEN])
        w2_sb = sb("w2_sb", [P, CHUNKS, DIM])
        rope_sb = sb("rope_sb", [P, 2, HEAD_DIM])
        mask_sb = sb("mask_sb", [P, HEADS])
        ident = sb("ident", [P, P])
        condT = sb("condT", [P, BATCH])
        scaleT = sb("scaleT", [P, BATCH])
        offT = sb("offT", [P, BATCH])
        eps_sb = sb("eps_sb", [P, TILES])
        half_neg = sb("half_neg", [P, TILES])
        stats_x = sb("stats_x", [P, TILES, 6])
        mv_x = sb("mv_x", [P, TILES, 2])
        veps_x = sb("veps_x", [P, TILES])
        rstd_x = sb("rstd_x", [P, TILES])
        shift_x = sb("shift_x", [P, TILES])
        stats = [sb(f"stats{u}", [P, ST, 6]) for u in range(2)]
        mv = [sb(f"mv{u}", [P, ST, 2]) for u in range(2)]
        veps = [sb(f"veps{u}", [P, ST]) for u in range(2)]
        rstd = [sb(f"rstd{u}", [P, ST]) for u in range(2)]
        xn = sb("xn", [P, ST, DIM])
        hs = sb("hs", [P, ST_TOKENS])
        hT = [sb(f"hT{u}", [P, ST_TOKENS]) for u in range(2)]
        rope_a = sb("rope_a", [P, ST * 2 * DIM])
        rope_b = sb("rope_b", [P, ST * 2 * DIM])
        qk_rot = sb("qk_rot", [P, ST * 2 * DIM])
        qT = [sb(f"qT{u}", [P, ST_TOKENS]) for u in range(2)]
        kT = sb("kT", [P, ST_TOKENS])
        k_spread = [sb(f"k_spread{u}", [P, HEADS, ST_TOKENS]) for u in range(2)]
        v_diag = [sb(f"v_diag{u}", [P, ST, TILE_BATCHES, HEADS, V_COLS]) for u in range(2)]
        neg_max = [sb(f"neg_max{u}", [P, HEADS]) for u in range(2)]
        shifted = [sb(f"shifted{u}", [P, HEADS * SEQ]) for u in range(2)]
        expd = [sb(f"expd{u}", [P, HEADS * SEQ]) for u in range(2)]
        eT = [sb(f"eT{u}", [P, HEADS * SEQ]) for u in range(2)]
        recip = sb("recip", [P, ST * HEADS])
        y_sb = sb("y_sb", [P, ST_TOKENS])
        yT = sb("yT", [P, ST_TOKENS])
        gelu = [sb(f"gelu{u}", [P, CHUNKS, ST_TOKENS]) for u in range(2)]

        bank_t = pb("bank_t", 512)
        bank_v = pb("bank_v", 512)
        bank_qk = pb("bank_qk", 1024)
        bank_log = [pb(f"bank_log{u}", 512) for u in range(2)]
        bank_pv = [pb(f"bank_pv{u}", 512) for u in range(2)]
        hidden_bank = [bank_qk[:, 0:512], bank_qk[:, 512:1024], bank_log[0][:, :], bank_log[1][:, :]]

        s_x_first = sem("x_first")
        s_x_rest = sem("x_rest")
        s_setup = sem("setup_loaded")
        s_attn_w = sem("attn_weights_loaded")
        s_mlp_w = sem("mlp_weights_loaded")
        s_half = sem("exponent_set")
        s_vzero = sem("v_diag_zeroed")
        s_vones = sem("v_diag_ones")
        s_condT_ps = sem("condT_in_psum")
        s_condT = sem("condT_ready")
        s_mod_ps = sem("modulation_in_psum")
        s_mod = sem("modulation_ready")
        s_w1s = sem("w1_scaled")
        s_stats = sem("stats_done")
        s_mv = sem("mean_var_done")
        s_veps = sem("var_eps_done")
        s_rstd = sem("rstd_ready")
        s_nshift = sem("norm_shift_ready")
        s_xn = sem("normed_ready")
        s_xnT = sem("normedT_in_psum")
        s_hs = sem("scaled_ready")
        s_hT = sem("hT_ready")
        s_qk = sem("qk_in_psum")
        s_v = sem("v_in_psum")
        s_rope = sem("rope_products_ready")
        s_rot = sem("qk_rotated")
        s_qkT = sem("qkT_in_psum")
        s_qT = sem("qT_ready")
        s_kT = sem("kT_ready")
        s_spread_a = sem("k_spread_by_act")
        s_spread_p = sem("k_spread_by_pool")
        s_vd = sem("v_diag_ready")
        s_log = sem("logits_in_psum")
        s_max = sem("max_done")
        s_shift = sem("logits_shifted")
        s_exp = sem("exp_done")
        s_eT = sem("expT_ready")
        s_pv = sem("pv_in_psum")
        s_recip = sem("recip_done")
        s_y = sem("y_normalised")
        s_yT = sem("yT_ready")
        s_wo = sem("proj_in_psum")
        s_x1 = sem("x1_ready")
        b_stats = sem("mlp_stats_done")
        b_mv = sem("mlp_mean_var_done")
        b_veps = sem("mlp_var_eps_done")
        b_rstd = sem("mlp_rstd_ready")
        b_n = sem("mlp_normed_ready")
        b_nT_ps = sem("mlp_normedT_in_psum")
        b_nT = sem("mlp_normedT_ready")
        b_h = sem("hidden_in_psum")
        b_g = sem("gelu_ready")
        b_o = sem("mlp_out_in_psum")
        b_res = sem("result_ready")
        s_store = sem("result_stored")

        x_t = x.rearrange("(t b) l d -> (b l) t d", b=TILE_BATCHES)
        out_t = out.rearrange("(t b) l d -> (b l) t d", b=TILE_BATCHES)

        block = ctx.enter_context(nc.Block())

        @block.sync
        def _(sp):
            sp.dma_start(x_sb[:, 0:ST, :], x_t[:, 0:ST, :]).then_inc(s_x_first, 16)
            sp.dma_start(ident[:, :], identity).then_inc(s_setup, 16)
            sp.dma_start(cond_sb[:, :], cond).then_inc(s_setup, 16)
            sp.dma_start(wsc_sb[:, :], w_scale).then_inc(s_setup, 16)
            sp.dma_start(wof_sb[:, :], w_offset).then_inc(s_setup, 16)
            sp.dma_start(wqk_sb[:, :], wqk).then_inc(s_attn_w, 16)
            sp.dma_start(wv_sb[:, :], wv).then_inc(s_attn_w, 16)
            sp.dma_start(rope_sb[:, :, :], rope).then_inc(s_attn_w, 16)
            sp.dma_start(mask_sb[:, :], head_mask).then_inc(s_attn_w, 16)
            sp.dma_start(wo_sb[:, :], wo).then_inc(s_attn_w, 16)
            sp.dma_start(x_sb[:, ST:TILES, :], x_t[:, ST:TILES, :]).then_inc(s_x_rest, 16)
            sp.dma_start(w1_sb[:, :], w1).then_inc(s_mlp_w, 16)
            sp.dma_start(lns_sb[:, :], ln_scale).then_inc(s_mlp_w, 16)
            sp.dma_start(w2_sb[:, :, :], w2.rearrange("(c p) n -> p c n", p=P)).then_inc(s_mlp_w, 16)
            with sp.Fori(0, STEPS) as g:
                sp.wait_ge(b_res, g + 1)
                sp.dma_start(out_t[:, bass.ds(ST * g, ST), :],
                             x1_sb[:, bass.ds(ST * g, ST), :]).then_inc(s_store, 16)
            sp.wait_ge(s_store, 16 * STEPS)

        @block.vector
        def _(dve):
            def x_statistics(m0, m1, count):
                tiles = range(ST * m0, ST * m1)
                for t in tiles:
                    last = nc.vector.bn_stats(stats_x[:, t, :], x_sb[:, t, :])
                last.then_inc(s_stats, 1)
                dve.wait_ge(s_stats, count)
                for t in tiles:
                    last = nc.vector.bn_aggr(mv_x[:, t, :], stats_x[:, t, :])
                last.then_inc(s_mv, 1)

            def x_shift(m0, m1, count):
                k = slice(ST * m0, ST * m1)
                dve.wait_ge(s_rstd, count)
                nc.vector.scalar_tensor_tensor(shift_x[:, k].unsqueeze(2), mv_x[:, k, 0:1], -1.0,
                                               rstd_x[:, k].unsqueeze(2), ALU.mult, ALU.mult).then_inc(s_nshift, 1)

            def modulate(m):
                dve.wait_ge(s_xnT, m + 1)
                dve.wait_ge(s_hT, m)
                nc.vector.tensor_tensor(
                    hs[:, :].rearrange("p (b l) -> p b l", l=SEQ),
                    bank_t[:, :].rearrange("p (b l) -> p b l", l=SEQ),
                    scaleT[:, bass.ds(ST_BATCHES * m, ST_BATCHES)].unsqueeze(2).to_broadcast([P, ST_BATCHES, SEQ]),
                    ALU.mult).then_inc(s_hs, 1)

            rope_n = ST * 2 * HEADS
            rope_src = bank_qk[:, :].rearrange("p (n d) -> p n d", d=HEAD_DIM)

            def rotate_cos(m):
                dve.wait_ge(s_qk, m + 1)
                dve.wait_ge(s_rot, m)
                nc.vector.tensor_tensor(rope_a[:, :].rearrange("p (n d) -> p n d", d=HEAD_DIM), rope_src,
                                        rope_sb[:, 0:1, :].to_broadcast([P, rope_n, HEAD_DIM]), ALU.mult)

            def rotate_sin(m):
                b = rope_b[:, :].rearrange("p (n d) -> p n d", d=HEAD_DIM)
                nc.vector.tensor_tensor(b[:, :, 0:HALF], rope_src[:, :, HALF:HEAD_DIM],
                                        rope_sb[:, 1:2, 0:HALF].to_broadcast([P, rope_n, HALF]), ALU.mult)
                nc.vector.tensor_tensor(b[:, :, HALF:HEAD_DIM], rope_src[:, :, 0:HALF],
                                        rope_sb[:, 1:2, HALF:HEAD_DIM].to_broadcast([P, rope_n, HALF]),
                                        ALU.mult).then_inc(s_rope, 1)

            def shift(m, t):
                src = bank_log[t % 2][:, :].rearrange("p (h k) -> p h k", k=SEQ)
                dve.wait_ge(s_log, ST * m + t + 1)
                nc.vector.tensor_reduce(neg_max[t % 2][:, :], src, axis=AX_X, op=ALU.max,
                                        negate=True).then_inc(s_max, 1)
                if t >= 2:
                    dve.wait_ge(s_exp, ST * m + t - 1)
                else:
                    dve.wait_ge(s_exp, ST * m)
                dve.wait_ge(s_max, ST * m + t + 1)
                nc.vector.tensor_tensor(shifted[t % 2][:, :].rearrange("p (h k) -> p h k", k=SEQ), src,
                                        neg_max[t % 2][:, :].unsqueeze(2).to_broadcast([P, HEADS, SEQ]),
                                        ALU.add).then_inc(s_shift, 1)

            def transpose_exp(m, t):
                dve.wait_ge(s_exp, ST * m + t + 1)
                if t >= 2:
                    dve.wait_ge(s_pv, ST * m + t - 1)
                else:
                    dve.wait_ge(s_pv, ST * m)
                nc.vector.transpose(eT[t % 2][:, :], expd[t % 2][:, :]).then_inc(s_eT, 1)

            def divide(m, pair):
                n = 2 * TILE_BATCHES * 4
                src = bank_pv[pair][:, 0:n * V_COLS].rearrange("p (n c) -> p n c", c=V_COLS)
                rec = recip[:, n * pair:n * (pair + 1)]
                dve.wait_ge(s_pv, ST * m + 2 * pair + 2)
                nc.vector.reciprocal(rec.unsqueeze(2), src[:, :, HEAD_DIM:V_COLS]).then_inc(s_recip, 1)
                dve.wait_ge(s_recip, 2 * m + pair + 1)
                nc.vector.tensor_tensor(
                    y_sb[:, 2 * P * pair:2 * P * (pair + 1)].rearrange("p (n d) -> p n d", d=HEAD_DIM),
                    src[:, :, 0:HEAD_DIM], rec.unsqueeze(2).to_broadcast([P, n, HEAD_DIM]),
                    ALU.mult).then_inc(s_y, 1)

            def transpose_y(m):
                dve.wait_ge(s_y, 2 * m + 2)
                nc.vector.transpose(yT[:, :], y_sb[:, :]).then_inc(s_yT, 1)

            def residual(m):
                dve.wait_ge(s_wo, m + 1)
                nc.vector.tensor_tensor(x1_sb[:, bass.ds(ST * m, ST), :],
                                        bank_t[:, :].rearrange("p (t d) -> p t d", d=DIM),
                                        x_sb[:, bass.ds(ST * m, ST), :], ALU.add).then_inc(s_x1, 1)

            def body(m, behind, ahead2, ahead3):
                shift(m, 0)
                transpose_exp(m, 0)
                shift(m, 1)
                if behind:
                    divide(m - 1, 1)
                    transpose_y(m - 1)
                transpose_exp(m, 1)
                shift(m, 2)
                if ahead3:
                    modulate(m + 3)
                if ahead2:
                    rotate_cos(m + 2)
                transpose_exp(m, 2)
                shift(m, 3)
                if ahead2:
                    rotate_sin(m + 2)
                if behind:
                    residual(m - 1)
                divide(m, 0)
                transpose_exp(m, 3)

            nc.vector.memset(eps_sb[:, :], EPS).then_inc(s_half, 1)
            nc.vector.memset(half_neg[:, :], -0.5).then_inc(s_half, 1)
            dve.wait_ge(s_x_first, 16)
            x_statistics(0, 1, 1)
            dve.wait_ge(s_condT_ps, 1)
            nc.vector.tensor_copy(condT[:, :], bank_pv[0][:, 0:BATCH]).then_inc(s_condT, 1)
            dve.wait_ge(s_vzero, 2)
            for u in range(2):
                for b in range(TILE_BATCHES):
                    last = nc.vector.memset(
                        v_diag[u][SEQ * b:SEQ * (b + 1), :, b, :, HEAD_DIM:V_COLS], 1.0)
            last.then_inc(s_vones, 1)
            x_shift(0, 1, 1)
            dve.wait_ge(s_mod_ps, 2)
            nc.vector.tensor_copy(scaleT[:, :], bank_pv[0][:, 0:BATCH]).then_inc(s_mod, 1)
            nc.vector.tensor_copy(offT[:, :], bank_pv[0][:, BATCH:2 * BATCH]).then_inc(s_mod, 1)
            dve.wait_ge(s_mod, 2)
            modulate(0)
            dve.wait_ge(s_x_rest, 16)
            x_statistics(1, 3, 2)
            dve.wait_ge(s_attn_w, 80)
            rotate_cos(0)
            rotate_sin(0)
            x_shift(1, 3, 2)
            x_statistics(3, 5, 3)
            modulate(1)
            x_shift(3, 5, 3)
            x_statistics(5, STEPS, 4)
            rotate_cos(1)
            rotate_sin(1)
            modulate(2)
            body(0, False, True, True)
            x_shift(5, STEPS, 4)
            with dve.Fori(0, 2) as i:
                for u in range(2):
                    body(2 * i + 1 + u, True, True, True)
            body(STEPS - 3, True, True, False)
            body(STEPS - 2, True, False, False)
            body(STEPS - 1, True, False, False)
            divide(STEPS - 1, 1)
            transpose_y(STEPS - 1)
            residual(STEPS - 1)

            def norm_stats(g, u):
                for t in range(ST):
                    last = nc.vector.bn_stats(stats[u][:, t, :], x1_sb[:, ST * g + t, :])
                last.then_inc(b_stats, 1)

            def norm_aggregate(u):
                for t in range(ST):
                    last = nc.vector.bn_aggr(mv[u][:, t, :], stats[u][:, t, :])
                last.then_inc(b_mv, 1)

            def mlp_normalise(g, u):
                dve.wait_ge(b_rstd, g + 1)
                dve.wait_ge(b_nT_ps, g)
                for t in range(ST):
                    last = nc.vector.tensor_scalar(xn[:, t, :], x1_sb[:, ST * g + t, :], mv[u][:, t, 0:1],
                                                   rstd[u][:, t:t + 1], ALU.subtract, ALU.mult)
                last.then_inc(b_n, 1)

            def mlp_norm(g, u):
                norm_stats(g, u)
                dve.wait_ge(b_stats, g + 1)
                norm_aggregate(u)
                mlp_normalise(g, u)

            def mlp_residual(g, u):
                dve.wait_ge(b_o, g + 1)
                nc.vector.tensor_tensor(x1_sb[:, bass.ds(ST * g, ST), :], bank_pv[u][:, :].rearrange("p (t d) -> p t d", d=DIM),
                                        x1_sb[:, bass.ds(ST * g, ST), :], ALU.add).then_inc(b_res, 1)

            dve.wait_ge(s_mlp_w, 48)
            nc.vector.tensor_scalar(w1s_sb[:, :], w1_sb[:, :], lns_sb[:, 0:1], None, ALU.mult).then_inc(s_w1s, 1)
            dve.wait_ge(s_x1, STEPS)
            for g in range(3):
                mlp_norm(g, g % 2)
            norm_stats(3, 1)
            dve.wait_ge(b_stats, 4)
            norm_aggregate(1)
            with dve.Fori(0, STEPS // 2 - 2) as i:
                for u in range(2):
                    g = 2 * i + u
                    norm_stats(g + 4, u)
                    dve.wait_ge(b_stats, g + 5)
                    mlp_residual(g, u)
                    norm_aggregate(u)
                    mlp_normalise(g + 3, 1 - u)
            mlp_normalise(STEPS - 1, 1)
            for g in range(STEPS - 4, STEPS):
                mlp_residual(g, g % 2)

        @block.gpsimd
        def _(pool):
            def x_inv_sigma(m0, m1, count):
                k = slice(ST * m0, ST * m1)
                pool.wait_ge(s_mv, count)
                nc.gpsimd.tensor_tensor(veps_x[:, k].unsqueeze(2), mv_x[:, k, 1:2], eps_sb[:, k].unsqueeze(2),
                                        ALU.add).then_inc(s_veps, 1)
                pool.wait_ge(s_veps, count)
                nc.gpsimd.tensor_tensor(rstd_x[:, k], veps_x[:, k], half_neg[:, k], ALU.pow).then_inc(s_rstd, 1)

            def inv_sigma(g, u):
                pool.wait_ge(b_mv, g + 1)
                nc.gpsimd.tensor_tensor(veps[u][:, :].unsqueeze(2), mv[u][:, :, 1:2], eps_sb[:, 0:ST].unsqueeze(2),
                                        ALU.add).then_inc(b_veps, 1)
                pool.wait_ge(b_veps, g + 1)
                nc.gpsimd.tensor_tensor(rstd[u][:, :], veps[u][:, :], half_neg[:, 0:ST], ALU.pow).then_inc(b_rstd, 1)

            def add_offset(m, u, reuse):
                pool.wait_ge(s_hs, m + 1)
                if reuse:
                    pool.wait_ge(s_v, m - 1)
                nc.gpsimd.tensor_tensor(
                    hT[u][:, :].rearrange("p (b l) -> p b l", l=SEQ),
                    hs[:, :].rearrange("p (b l) -> p b l", l=SEQ),
                    offT[:, bass.ds(ST_BATCHES * m, ST_BATCHES)].unsqueeze(2).to_broadcast([P, ST_BATCHES, SEQ]),
                    ALU.add).then_inc(s_hT, 1)

            def rotate_add(m):
                pool.wait_ge(s_rope, m + 1)
                pool.wait_ge(s_qkT, m)
                nc.gpsimd.tensor_tensor(qk_rot[:, :], rope_a[:, :], rope_b[:, :], ALU.add).then_inc(s_rot, 1)

            def spread(m, u, reuse):
                pool.wait_ge(s_kT, m + 1)
                if reuse:
                    pool.wait_ge(s_log, ST * (m - 1))
                nc.gpsimd.tensor_tensor(k_spread[u][:, ACT_HEADS, :], kT[:, :],
                                        mask_sb[:, ACT_HEADS:ACT_HEADS + 1].to_broadcast([P, ST_TOKENS]), ALU.mult)
                for h in range(ACT_HEADS + 1, HEADS):
                    last = nc.gpsimd.tensor_scalar(k_spread[u][:, h, :], kT[:, :], mask_sb[:, h:h + 1], 0.0,
                                                   ALU.mult, ALU.add)
                last.then_inc(s_spread_p, 1)

            def body(m, u, reuse, ahead2, ahead3):
                rotate_add(m + 1)
                spread(m + 1, 1 - u, reuse)
                if ahead3:
                    add_offset(m + 3, 1 - u, True)

            for u in range(2):
                nc.gpsimd.memset(v_diag[u][:, :, :, :, :], 0.0).then_inc(s_vzero, 1)
            pool.wait_ge(s_half, 2)
            x_inv_sigma(0, 1, 1)
            pool.wait_ge(s_mod, 2)
            add_offset(0, 0, False)
            x_inv_sigma(1, 3, 2)
            rotate_add(0)
            x_inv_sigma(3, 5, 3)
            pool.wait_ge(s_attn_w, 80)
            add_offset(1, 1, False)
            spread(0, 0, False)
            add_offset(2, 0, True)
            rotate_add(1)
            x_inv_sigma(5, STEPS, 4)
            spread(1, 1, False)
            add_offset(3, 1, True)
            with pool.Fori(0, 2) as i:
                for u in range(2):
                    body(2 * i + 1 + u, 1 - u, True, True, True)
            body(STEPS - 3, 1, True, True, False)
            body(STEPS - 2, 0, True, False, False)

            with pool.Fori(0, STEPS // 2) as i:
                for u in range(2):
                    inv_sigma(2 * i + u, u)

        @block.scalar
        def _(act):
            def normalise(m):
                act.wait_ge(s_xnT, m)
                for t in range(ST):
                    k = ST * m + t
                    last = nc.scalar.activation(xn[:, t, :], x_sb[:, k, :], ACT.Identity,
                                                bias=shift_x[:, bass.ds(k, 1)], scale=rstd_x[:, bass.ds(k, 1)])
                last.then_inc(s_xn, 1)

            def place_v(m, u, reuse):
                act.wait_ge(s_v, m + 1)
                if reuse:
                    act.wait_ge(s_pv, ST * (m - 1))
                for b in range(TILE_BATCHES):
                    rows = slice(SEQ * b, SEQ * (b + 1))
                    last = nc.scalar.activation(
                        v_diag[u][rows, :, b, :, 0:HEAD_DIM],
                        bank_v[rows, :].rearrange("p (t h d) -> p t h d", h=HEADS, d=HEAD_DIM), ACT.Copy)
                last.then_inc(s_vd, 1)

            def evict_qkT(m, u, reuse):
                act.wait_ge(s_qkT, m + 1)
                if reuse:
                    act.wait_ge(s_log, ST * (m - 1))
                nc.scalar.activation(qT[u][:, :], bank_qk[:, 0:512], ACT.Copy,
                                     scale=float(DIM) ** -0.5).then_inc(s_qT, 1)
                act.wait_ge(s_spread_p, m)
                act.wait_ge(s_spread_a, m)
                nc.scalar.activation(kT[:, :], bank_qk[:, 512:1024], ACT.Copy).then_inc(s_kT, 1)

            def spread(m, u, first, last_head):
                if first == 0:
                    act.wait_ge(s_kT, m + 1)
                for h in range(first, last_head):
                    last = nc.scalar.activation(k_spread[u][:, h, :], kT[:, :], ACT.Copy,
                                                scale=mask_sb[:, h:h + 1])
                if last_head == ACT_HEADS:
                    last.then_inc(s_spread_a, 1)

            def exponentiate(m, t):
                act.wait_ge(s_shift, ST * m + t + 1)
                if t >= 2:
                    act.wait_ge(s_eT, ST * m + t - 1)
                else:
                    act.wait_ge(s_eT, ST * m)
                nc.scalar.activation(expd[t % 2][:, :], shifted[t % 2][:, :], ACT.Exp).then_inc(s_exp, 1)

            act.wait_ge(s_nshift, 1)
            normalise(0)
            act.wait_ge(s_vones, 1)
            place_v(0, 0, False)
            act.wait_ge(s_nshift, 2)
            normalise(1)
            act.wait_ge(s_attn_w, 80)
            evict_qkT(0, 0, False)
            normalise(2)
            spread(0, 0, 0, ACT_HEADS)
            def body(m, u, reuse, ahead3):
                exponentiate(m, 0)
                evict_qkT(m + 1, 1 - u, reuse)
                if ahead3:
                    normalise(m + 3)
                exponentiate(m, 1)
                spread(m + 1, 1 - u, 0, 2)
                place_v(m + 1, 1 - u, reuse)
                exponentiate(m, 2)
                spread(m + 1, 1 - u, 2, ACT_HEADS)
                exponentiate(m, 3)

            act.wait_ge(s_nshift, 3)
            body(0, 0, False, True)
            act.wait_ge(s_nshift, 4)
            with act.Fori(0, 2) as i:
                for u in range(2):
                    body(2 * i + 1 + u, 1 - u, True, True)
            body(STEPS - 3, 1, True, False)
            body(STEPS - 2, 0, True, False)
            for t in range(ST):
                exponentiate(STEPS - 1, t)

            def evict_nT(g):
                act.wait_ge(b_nT_ps, g + 1)
                act.wait_ge(b_h, CHUNKS * g)
                nc.scalar.activation(hT[0][:, :], bank_t[:, :], ACT.Copy).then_inc(b_nT, 1)

            def gelus(g, u, reuse):
                for c in range(CHUNKS):
                    act.wait_ge(b_h, CHUNKS * g + c + 1)
                    if reuse and c == 0:
                        act.wait_ge(b_o, g - 1)
                    nc.scalar.activation(gelu[u][:, c, :], hidden_bank[c], ACT.Gelu_apprx_tanh).then_inc(b_g, 1)

            act.wait_ge(s_v, STEPS)
            evict_nT(0)
            gelus(0, 0, False)
            evict_nT(1)
            gelus(1, 1, False)
            with act.Fori(1, STEPS // 2) as i:
                for u in range(2):
                    evict_nT(2 * i + u)
                    gelus(2 * i + u, u, True)

        @block.tensor
        def _(pe):
            def transpose_norm(m, projected):
                pe.wait_ge(s_xn, m + 1)
                pe.wait_ge(s_hs, m)
                if projected:
                    pe.wait_ge(s_shift, ST * (m - 3))
                for t in range(ST):
                    last = nc.tensor.transpose(bank_t[:, P * t:P * (t + 1)], xn[:, t, :], ident[:, :])
                last.then_inc(s_xnT, 1)

            def project_qk(m, u):
                pe.wait_ge(s_hT, m + 1)
                pe.wait_ge(s_kT, m)
                pe.wait_ge(s_qT, m)
                for t in range(ST):
                    last = nc.tensor.matmul(bank_qk[:, 2 * DIM * t:2 * DIM * (t + 1)], hT[u][:, P * t:P * (t + 1)],
                                            wqk_sb[:, :], start=True, stop=True)
                last.then_inc(s_qk, 1)

            def project_v(m, u):
                pe.wait_ge(s_vd, m)
                for t in range(ST):
                    last = nc.tensor.matmul(bank_v[:, DIM * t:DIM * (t + 1)], hT[u][:, P * t:P * (t + 1)],
                                            wv_sb[:, :], start=True, stop=True)
                last.then_inc(s_v, 1)

            def transpose_qk(m):
                pe.wait_ge(s_rot, m + 1)
                for j in range(2):
                    for t in range(ST):
                        c = 2 * DIM * t + DIM * j
                        last = nc.tensor.transpose(bank_qk[:, 512 * j + P * t:512 * j + P * (t + 1)],
                                                   qk_rot[:, c:c + DIM], ident[:, :])
                last.then_inc(s_qkT, 1)

            def logits(m, u, t):
                if t == 0:
                    pe.wait_ge(s_qT, m + 1)
                    pe.wait_ge(s_spread_a, m + 1)
                    pe.wait_ge(s_spread_p, m + 1)
                if t >= 2:
                    pe.wait_ge(s_shift, ST * m + t - 1)
                else:
                    pe.wait_ge(s_shift, ST * m)
                for b in range(TILE_BATCHES):
                    c = P * t + SEQ * b
                    last = nc.tensor.matmul(bank_log[t % 2][SEQ * b:SEQ * (b + 1), :], qT[u][:, c:c + SEQ],
                                            k_spread[u][:, :, c:c + SEQ], start=True, stop=True)
                last.then_inc(s_log, 1)

            def first_y(m):
                return 0 if isinstance(m, int) and m == 0 else 2 * m - 1

            def weigh(m, u, t):
                if t == 0:
                    pe.wait_ge(s_vd, m + 1)
                    pe.wait_ge(s_y, first_y(m))
                if t == 2:
                    pe.wait_ge(s_y, 2 * m)
                pe.wait_ge(s_eT, ST * m + t + 1)
                for g in range(4):
                    for j in range(4):
                        h = 4 * j + g
                        base = (t % 2) * TILE_BATCHES * 4 * V_COLS
                        dst = bank_pv[t // 2][SEQ * j:SEQ * (j + 1), base:base + TILE_BATCHES * 4 * V_COLS]
                        dst = dst.rearrange("p (b g c) -> p b g c", b=TILE_BATCHES, g=4)[:, :, g, :]
                        last = nc.tensor.matmul(dst, eT[t % 2][:, SEQ * h:SEQ * (h + 1)],
                                                v_diag[u][:, t, :, h, :], start=True, stop=True)
                last.then_inc(s_pv, 1)

            def project_out(m, ahead):
                pe.wait_ge(s_yT, m + 1)
                if ahead:
                    pe.wait_ge(s_hs, m + 5)
                else:
                    pe.wait_ge(s_x1, m)
                for t in range(ST):
                    last = nc.tensor.matmul(bank_t[:, DIM * t:DIM * (t + 1)], yT[:, P * t:P * (t + 1)],
                                            wo_sb[:, :], start=True, stop=True)
                last.then_inc(s_wo, 1)

            def body(m, u, behind, ahead1, ahead2, ahead3):
                logits(m, u, 1)
                if ahead1:
                    transpose_qk(m + 1)
                if behind:
                    weigh(m - 1, 1 - u, 3)
                logits(m, u, 2)
                if ahead3:
                    transpose_norm(m + 3, behind)
                weigh(m, u, 0)
                if ahead2:
                    project_qk(m + 2, u)
                logits(m, u, 3)
                weigh(m, u, 1)
                if ahead2:
                    project_v(m + 2, u)
                if behind:
                    project_out(m - 1, ahead3)
                if ahead1:
                    logits(m + 1, 1 - u, 0)
                weigh(m, u, 2)

            pe.wait_ge(s_setup, 64)
            nc.tensor.transpose(bank_pv[0][:, 0:BATCH], cond_sb[:, :], ident[:, :]).then_inc(s_condT_ps, 1)
            pe.wait_ge(s_condT, 1)
            nc.tensor.matmul(bank_pv[0][:, 0:BATCH], wsc_sb[:, :], condT[:, :], start=True,
                             stop=True).then_inc(s_mod_ps, 1)
            nc.tensor.matmul(bank_pv[0][:, BATCH:2 * BATCH], wof_sb[:, :], condT[:, :], start=True,
                             stop=True).then_inc(s_mod_ps, 1)
            transpose_norm(0, False)
            pe.wait_ge(s_attn_w, 80)
            project_qk(0, 0)
            project_v(0, 0)
            transpose_norm(1, False)
            transpose_qk(0)
            project_qk(1, 1)
            project_v(1, 1)
            transpose_norm(2, False)
            logits(0, 0, 0)
            body(0, 0, False, True, True, True)
            with pe.Fori(0, 2) as i:
                for u in range(2):
                    body(2 * i + 1 + u, 1 - u, True, True, True, True)
            body(STEPS - 3, 1, True, True, True, False)
            body(STEPS - 2, 0, True, True, False, False)
            body(STEPS - 1, 1, True, False, False, False)
            weigh(STEPS - 1, 1, 3)
            project_out(STEPS - 1, False)

            def transpose_mlp_norm(g):
                pe.wait_ge(b_n, g + 1)
                pe.wait_ge(b_nT, g)
                for t in range(ST):
                    last = nc.tensor.transpose(bank_t[:, P * t:P * (t + 1)], xn[:, t, :], ident[:, :])
                last.then_inc(b_nT_ps, 1)

            def hidden(g):
                pe.wait_ge(b_nT, g + 1)
                for c in range(CHUNKS):
                    pe.wait_ge(b_g, CHUNKS * g)
                    nc.tensor.matmul(hidden_bank[c], w1s_sb[:, P * c:P * (c + 1)], hT[0][:, :], start=True,
                                     stop=True).then_inc(b_h, 1)

            def down(g, u, reuse):
                pe.wait_ge(b_g, CHUNKS * (g + 1))
                if reuse:
                    pe.wait_ge(b_res, g - 1)
                for t in range(ST):
                    for c in range(CHUNKS):
                        last = nc.tensor.matmul(bank_pv[u][:, DIM * t:DIM * (t + 1)],
                                                gelu[u][:, c, P * t:P * (t + 1)], w2_sb[:, c, :],
                                                start=(c == 0), stop=(c == CHUNKS - 1))
                last.then_inc(b_o, 1)

            pe.wait_ge(s_mlp_w, 48)
            pe.wait_ge(s_w1s, 1)
            transpose_mlp_norm(0)
            hidden(0)
            transpose_mlp_norm(1)
            for g in range(2):
                hidden(g + 1)
                transpose_mlp_norm(g + 2)
                down(g, g, False)
            with pe.Fori(1, STEPS // 2 - 1) as i:
                for u in range(2):
                    g = 2 * i + u
                    hidden(g + 1)
                    transpose_mlp_norm(g + 2)
                    down(g, u, True)
            hidden(STEPS - 1)
            down(STEPS - 2, 0, True)
            down(STEPS - 1, 1, True)


def _constants():
    freq = 10000.0 ** (-np.arange(0, HEAD_DIM, 2, dtype=np.float32) / HEAD_DIM)
    grid = (np.arange(P, dtype=np.float32) % SEQ)[:, None] * freq[None, :].astype(np.float32)
    cos, sin = np.cos(grid).astype(np.float32), np.sin(grid).astype(np.float32)
    rope = np.stack([np.concatenate([cos, cos], 1), np.concatenate([-sin, sin], 1)], 1)
    mask = (np.arange(P)[:, None] // HEAD_DIM == np.arange(HEADS)[None, :]).astype(np.float32)
    return np.ascontiguousarray(rope, np.float32), mask, np.eye(P, dtype=np.float32)


def kernel(**inputs):
    import concourse.bacc as bacc
    from concourse.bass_utils import run_bass_kernel_spmd as run

    pre = "L0_cond_"
    order = np.concatenate([h * HEAD_DIM + np.concatenate([np.arange(0, HEAD_DIM, 2), np.arange(1, HEAD_DIM, 2)])
                            for h in range(HEADS)])
    wq, wk = (np.asarray(inputs[pre + n])[:, order] for n in ("wq", "wk"))
    rope, mask, eye = _constants()
    arrays = {
        "x_in": np.asarray(inputs["x"]),
        "cond_in": np.asarray(inputs["cond_1024"]),
        "w_scale_in": np.asarray(inputs[pre + "w_scale"]),
        "w_offset_in": np.asarray(inputs[pre + "w_offset"]),
        "wqk_in": np.concatenate([wq, wk], 1),
        "wv_in": np.asarray(inputs[pre + "wv"]),
        "wo_in": np.asarray(inputs[pre + "wo"]),
        "ln_scale_in": np.asarray(inputs[pre + "mlp_ln_scale"]).reshape(DIM, 1),
        "w1_in": np.asarray(inputs[pre + "w1"]),
        "w2_in": np.asarray(inputs[pre + "w2"]),
        "rope_in": rope,
        "head_mask_in": mask,
        "identity_in": eye,
    }
    arrays = {n: np.ascontiguousarray(a) for n, a in arrays.items()}
    nc = bacc.Bacc("TRN2", target_bir_lowering=False, num_devices=1)
    args = [nc.dram_tensor(n, a.shape, mybir.dt.from_np(a.dtype), kind="ExternalInput").ap() for n, a in arrays.items()]
    out = nc.dram_tensor("block_out", (BATCH, SEQ, DIM), F32, kind="ExternalOutput").ap()
    build(nc, *args, out)
    r = run(nc, [arrays], core_ids=[0])
    return r.results[0]["block_out"]
```
